# Optimizing a Trainium2 kernel written in Bass

```python
import numpy as np
import jax
import jax.numpy as jnp

def _softmax(x, axis=-1):
    return jax.nn.softmax(x, axis=axis)

def _gelu(x):
    return jax.nn.gelu(x, approximate=True)

def _silu(x):
    return jax.nn.silu(x)

def _sigmoid(x):
    return jax.nn.sigmoid(x)

def _layernorm(x, axis=-1, eps=1e-05):
    m = jnp.mean(x, axis=axis, keepdims=True)
    v = jnp.var(x, axis=axis, keepdims=True)
    return (x - m) / jnp.sqrt(v + eps)

def _scatter_add(tgt, idx, src, axis=0):
    return tgt.at[idx].add(src)

def _segment_sum(src, seg, n):
    return jax.ops.segment_sum(src, seg, n)
kernel_name = 'mk_gnn_ffn_d1_gnn_r8_f8d392'

def setup_inputs(seed: int=0):
    np.random.seed(seed)
    _w = jnp.asarray

    def _rec_inputs():
        import jax
        import jax.numpy as jnp
        _gk = jax.random.key(seed)
        x = -0.0003713 + 1 * jax.random.normal(jax.random.fold_in(_gk, 1), (6250, 256), jnp.float32)
        src = jax.random.randint(jax.random.fold_in(_gk, 2), (200000,), 0, 6250, jnp.int32)
        dst = jnp.minimum((6250 * jax.random.uniform(jax.random.fold_in(_gk, 3), (200000,)) ** 2.0).astype(jnp.int32), 49999)
        _o = jnp.argsort(dst, stable=True)
        src = src[_o]
        dst = dst[_o]
        edge_weight = jax.random.uniform(jax.random.fold_in(_gk, 12), (200000,), jnp.float32, 0.0, 0.999998)
        return (x, src, dst, edge_weight)
    x, src, dst, edge_weight = _rec_inputs()

    def _L0_gnn_setup():
        import jax, jax.numpy as jnp
        import numpy as np
        N_NODES = 6250
        N_EDGES = 37500
        D = 256
        EPS = 1e-12

        def _gcn_layer(x, W, b, src, dst, norm, n_nodes):
            xt = x @ W
            msg = xt[src] * norm[:, None]
            agg = jax.ops.segment_sum(msg, dst, num_segments=n_nodes)
            return jax.nn.relu(agg + b)
        key = jax.random.key(seed)
        ks = jax.random.split(key, 10)
        h5_all = jax.random.normal(ks[0], (N_NODES, D), dtype=jnp.float32)
        edge_index = jax.random.randint(ks[1], (2, N_EDGES), 0, N_NODES, dtype=jnp.int64)
        edge_weight = jax.random.uniform(ks[2], (N_EDGES,), dtype=jnp.float32)
        s = 1.0 / np.sqrt(D)
        W6 = jax.random.normal(ks[3], (D, D), dtype=jnp.float32) * s
        b6 = jnp.zeros((D,), dtype=jnp.float32)
        W7 = jax.random.normal(ks[4], (D, D), dtype=jnp.float32) * s
        b7 = jnp.zeros((D,), dtype=jnp.float32)
        Wp = jax.random.normal(ks[5], (D, D), dtype=jnp.float32) * s
        bp = jnp.zeros((D,), dtype=jnp.float32)
        return {'h5_all': h5_all, 'edge_index': edge_index, 'edge_weight': edge_weight, 'W6': W6, 'b6': b6, 'W7': W7, 'b7': b7, 'Wp': Wp, 'bp': bp}
    _L0_gnn_all = _L0_gnn_setup()
    _L0_gnn_in = {k: v for k, v in _L0_gnn_all.items() if k in ('W6', 'b6', 'W7', 'b7', 'Wp', 'bp')}
    del _L0_gnn_all

    def _L0_ffn_setup():
        import jax, jax.numpy as jnp
        import numpy as np
        B, S, H, F, E, K = (8, 512, 256, 512, 16, 2)
        EPS = 1e-05
        key = jax.random.key(seed)
        ks = jax.random.split(key, 9)
        sc = 0.02
        return {'x': jax.random.normal(ks[0], (B, S, H), dtype=jnp.float32), 'gate_w': jax.random.normal(ks[1], (H, E), dtype=jnp.float32) * sc, 'gate_b': jnp.zeros((E,), dtype=jnp.float32), 'w1': jax.random.normal(ks[2], (E, H, F), dtype=jnp.float32) * sc, 'b1': jnp.zeros((E, F), dtype=jnp.float32), 'w2': jax.random.normal(ks[3], (E, F, H), dtype=jnp.float32) * sc, 'b2': jnp.zeros((E, H), dtype=jnp.float32), 'gamma': jnp.ones((H,), dtype=jnp.float32), 'beta': jnp.zeros((H,), dtype=jnp.float32)}
    _L0_ffn_all = _L0_ffn_setup()
    _L0_ffn_in = {k: v for k, v in _L0_ffn_all.items() if k in ('gate_w', 'gate_b', 'w1', 'b1', 'w2', 'b2', 'gamma', 'beta')}
    del _L0_ffn_all
    return {'x': x, 'src': src, 'dst': dst, 'edge_weight': edge_weight, 'L0_gnn_W6': _L0_gnn_in['W6'], 'L0_gnn_b6': _L0_gnn_in['b6'], 'L0_gnn_W7': _L0_gnn_in['W7'], 'L0_gnn_b7': _L0_gnn_in['b7'], 'L0_gnn_Wp': _L0_gnn_in['Wp'], 'L0_gnn_bp': _L0_gnn_in['bp'], 'L0_ffn_gate_w': _L0_ffn_in['gate_w'], 'L0_ffn_gate_b': _L0_ffn_in['gate_b'], 'L0_ffn_w1': _L0_ffn_in['w1'], 'L0_ffn_b1': _L0_ffn_in['b1'], 'L0_ffn_w2': _L0_ffn_in['w2'], 'L0_ffn_b2': _L0_ffn_in['b2'], 'L0_ffn_gamma': _L0_ffn_in['gamma'], 'L0_ffn_beta': _L0_ffn_in['beta']}

def reference(x, src, dst, edge_weight, L0_gnn_W6, L0_gnn_b6, L0_gnn_W7, L0_gnn_b7, L0_gnn_Wp, L0_gnn_bp, L0_ffn_gate_w, L0_ffn_gate_b, L0_ffn_w1, L0_ffn_b1, L0_ffn_w2, L0_ffn_b2, L0_ffn_gamma, L0_ffn_beta):
    import jax
    import jax.numpy as jnp

    def _L0_gnn_ref(h5_all, edge_index, edge_weight, W6, b6, W7, b7, Wp, bp):
        import jax, jax.numpy as jnp
        import numpy as np
        N_NODES = 6250
        N_EDGES = 37500
        D = 256
        EPS = 1e-12

        def _gcn_layer(x, W, b, src, dst, norm, n_nodes):
            xt = x @ W
            msg = xt[src] * norm[:, None]
            agg = jax.ops.segment_sum(msg, dst, num_segments=n_nodes)
            return jax.nn.relu(agg + b)
        src, dst = (edge_index[0], edge_index[1])
        deg_out = jax.ops.segment_sum(edge_weight, src, num_segments=N_NODES)
        deg_in = jax.ops.segment_sum(edge_weight, dst, num_segments=N_NODES)
        norm = edge_weight * jax.lax.rsqrt(deg_out[src] * deg_in[dst] + EPS)
        h6 = _gcn_layer(h5_all, W6, b6, src, dst, norm, N_NODES)
        h7 = _gcn_layer(h6, W7, b7, src, dst, norm, N_NODES)
        out = h7 @ Wp + bp
        return out

    def _L0_ffn_ref(x, gate_w, gate_b, w1, b1, w2, b2, gamma, beta):
        import jax, jax.numpy as jnp
        import numpy as np
        B, S, H, F, E, K = (8, 512, 256, 512, 16, 2)
        EPS = 1e-05
        gate_logits = x @ gate_w + gate_b
        topk_vals, topk_idx = jax.lax.top_k(gate_logits, K)
        topk_w = jax.nn.softmax(topk_vals, axis=-1)
        h = jax.nn.relu(jnp.einsum('bsh,ehf->bsef', x, w1) + b1)
        expert_out = jnp.einsum('bsef,efh->bseh', h, w2) + b2
        sel = jnp.take_along_axis(expert_out, topk_idx[:, :, :, None], axis=2)
        moe = jnp.sum(topk_w[..., None] * sel, axis=2)
        y = x + moe
        mu = jnp.mean(y, axis=-1, keepdims=True)
        var = jnp.var(y, axis=-1, keepdims=True)
        return (y - mu) / jnp.sqrt(var + EPS) * gamma + beta
    edge_index = jnp.stack([src, dst])
    x = x + _L0_gnn_ref(_layernorm(x, axis=-1), edge_index, edge_weight, L0_gnn_W6, L0_gnn_b6, L0_gnn_W7, L0_gnn_b7, L0_gnn_Wp, L0_gnn_bp)
    x = x + _L0_ffn_ref(_layernorm(x, axis=-1)[None], L0_ffn_gate_w, L0_ffn_gate_b, L0_ffn_w1, L0_ffn_b1, L0_ffn_w2, L0_ffn_b2, L0_ffn_gamma, L0_ffn_beta)[0]
    return x

_drawn_inputs = setup_inputs


def setup_inputs(seed=0):
    import zlib

    import numpy as np

    out = dict(_drawn_inputs(seed))
    spreads = {'L0_gnn_b6': (0.0, 0.1),
     'L0_gnn_b7': (0.0, 0.1),
     'L0_gnn_bp': (0.0, 0.1),
     'L0_ffn_gate_b': (0.0, 0.1),
     'L0_ffn_b1': (0.0, 0.705),
     'L0_ffn_b2': (0.0, 0.1),
     'L0_ffn_gamma': (1.0, 0.2),
     'L0_ffn_beta': (0.0, 0.1)}
    factors = {'edge_weight': 4.279, 'L0_gnn_W6': 3.066}
    for name, (base, spread) in spreads.items():
        noise = np.random.default_rng([zlib.crc32(name.encode()), seed]).standard_normal(out[name].shape)
        drawn = base * np.exp(spread * noise) if base else spread * noise
        out[name] = jnp.asarray(drawn.astype(out[name].dtype))
    for name, factor in factors.items():
        out[name] = (out[name] * factor).astype(out[name].dtype)
    return out
```

```python
from contextlib import ExitStack

import numpy as np

import concourse.bass as bass
from concourse import mybir

f32 = mybir.dt.float32
bf16 = mybir.dt.bfloat16
i32 = mybir.dt.int32
u32 = mybir.dt.uint32
ALU = mybir.AluOpType
ACT = mybir.ActivationFunctionType
AX = mybir.AxisListType
ds = bass.ds

P = 128
NODES, D, EDGES = 6250, 256, 200000
KD = D // P
NT = -(-NODES // P)
NP = NT + NT % 2
LAST = NODES - (NT - 1) * P
GT = 8
SLOTS = 4
GROUPS = -(-EDGES // (P * GT * SLOTS)) * SLOTS
ET = GROUPS * GT
EC = -(-ET // P)
FULL = EDGES // P
REST = EDGES - FULL * P
ROW = D + 4
PADDST = NT * P - 1
E, F, FC = 16, 512, 4
ST = (2 * NODES + E * (P - 1)) // P
ST += ST % 2
ST_BITS = 7
LN_EPS, GCN_EPS = 1e-5, 1e-12


class Steps:

    def __init__(self, engine, semaphore):
        self.engine, self.semaphore, self.count = engine, semaphore, 0

    def __call__(self, instruction):
        self.count += 1
        instruction.then_inc(self.semaphore, 1)
        self.engine.wait_ge(self.semaphore, self.count)


class Scope:

    def __init__(self, nc, name):
        self.nc, self.name, self.stack, self.semaphores = nc, name, ExitStack(), []

    def __enter__(self):
        return self

    def __exit__(self, *e):
        self.stack.close()
        if self.semaphores and e[0] is None:
            self.nc.clear_and_free_semaphores(self.semaphores)
            self.nc.all_engine_barrier()

    def sb(self, name, shape, dt=f32):
        return self.stack.enter_context(self.nc.sbuf_tensor(f"{self.name}_{name}", shape, dt))

    def ps(self, name, shape, dt=f32):
        return self.stack.enter_context(self.nc.psum_tensor(f"{self.name}_{name}", shape, dt))

    def sem(self, name):
        self.semaphores.append(self.nc.alloc_semaphore(f"{self.name}_{name}"))
        return self.semaphores[-1]

    def block(self):
        return self.stack.enter_context(self.nc.Block())


def constants(nc, c):
    with Scope(nc, "const") as s:
        filled, counted = s.sem("filled"), s.sem("counted")
        block = s.block()

        @block.gpsimd
        def _(pool):
            pool.memset(c["ident"][:, :], 0.0)
            pool.memset(c["tri"][:, :], 1.0)
            pool.memset(c["ones"][:, :], 1.0)
            pool.memset(c["eps_ln"][:, :], LN_EPS)
            pool.memset(c["eps_gcn"][:, :], GCN_EPS).then_inc(filled, 1)
            pool.wait_ge(filled, 1)
            pool.affine_select(out=c["ident"][:, :], in_=c["ident"][:, :], compare_op=ALU.not_equal, fill=1.0,
                               base=0, pattern=[[-1, P]], channel_multiplier=1)
            pool.affine_select(out=c["tri"][:, :], in_=c["tri"][:, :], compare_op=ALU.is_gt, fill=0.0,
                               base=0, pattern=[[1, P]], channel_multiplier=-1)
            pool.iota(c["iota"][:, :], pattern=[[1, P]], base=0, channel_multiplier=0,
                      allow_small_or_imprecise_dtypes=True)
            pool.iota(c["iota_bf"][:, :], pattern=[[1, P]], base=0, channel_multiplier=0,
                      allow_small_or_imprecise_dtypes=True)
            pool.iota(c["window"][:, :], pattern=[[P, NP]], base=0, channel_multiplier=0,
                      allow_small_or_imprecise_dtypes=True)
            pool.iota(c["token"][:, :], pattern=[[P, NP]], base=0, channel_multiplier=1,
                      allow_small_or_imprecise_dtypes=True).then_inc(counted, 1)
            pool.wait_ge(counted, 1)


def edge_tables(nc, c, src, dst, edge_weight, range_dram, srcf, dstf, wv, tab):
    with Scope(nc, "edge") as s:
        raw_i = s.sb("raw_i", [P, 2, EC, P], i32)
        raw_w = s.sb("raw_w", [P, EC, P])
        raw_f = s.sb("raw_f", [P, 2, EC, P])
        lohi = s.sb("lohi", [P, 2, EC])
        lohi_t = s.sb("lohi_t", [EC, 2, P // GT])
        NG = EC * (P // GT)
        rng = s.sb("rng", [1, 2, NG])
        rng_i = s.sb("rng_i", [1, 2, NG], i32)
        win = s.sb("win", [1, 2, NG])
        ones = s.sb("ones", [1, NG])
        passes = s.sb("passes", [1, NG])
        tab_f = s.sb("tab_f", [1, GROUPS, 4])
        tp = [s.ps(f"tp{i}", [P, 4, P]) for i in range(2)]
        tr = s.ps("tr", [EC, 2, P])
        padded, loaded, cast, ranged = s.sem("padded"), s.sem("loaded"), s.sem("cast"), s.sem("ranged")
        turned, copied, steps = s.sem("turned"), s.sem("copied"), s.sem("steps")
        range_turned, range_out, range_in, range_done = s.sem("rt"), s.sem("ro"), s.sem("ri"), s.sem("rd")
        block = s.block()
        lots = [(k, ch, min(4, EC - ch)) for k in range(3) for ch in range(0, EC, 4)]

        @block.gpsimd
        def _(pool):
            pool.memset(raw_i[:, 0, EC - 1, :], 0)
            pool.memset(raw_i[:, 1, EC - 1, :], PADDST)
            pool.memset(raw_w[:, EC - 1, :], 0.0).then_inc(padded, 1)
            pool.memset(srcf[:, ET:], 0.0)

        @block.sync
        def _(sp):
            sp.wait_ge(padded, 1)
            body = (EC - 1) * P
            for to, of in ((raw_i[:, 0], src), (raw_i[:, 1], dst), (raw_w, edge_weight)):
                sp.dma_start(to[:, 0:EC - 1, :], of[0:body * P].rearrange("(c p e) -> p c e", p=P, e=P)).then_inc(loaded, 16)
                sp.dma_start(to[0:FULL - body, EC - 1, :],
                             of[body * P:FULL * P].rearrange("(p e) -> p e", e=P)).then_inc(loaded, 16)
                sp.dma_start(to[FULL - body:FULL - body + 1, EC - 1, 0:REST],
                             of[FULL * P:EDGES].rearrange("(p e) -> p e", p=1)).then_inc(loaded, 16)
            sp.wait_ge(range_turned, 1)
            sp.dma_start(range_dram.rearrange("k (c g) -> c k g", g=P // GT), lohi_t[:, :, :]).then_inc(range_out, 16)
            sp.wait_ge(range_out, 16)
            sp.dma_start(rng[:, :, :], range_dram.rearrange("(a k) g -> a k g", a=1)).then_inc(range_in, 16)

        @block.vector
        def _(dve):
            step = Steps(dve, steps)
            dve.wait_ge(loaded, 16 * 9)
            nc.vector.tensor_copy(raw_f[:, 1], raw_i[:, 1]).then_inc(cast, 1)
            nc.vector.tensor_copy(raw_f[:, 0], raw_i[:, 0]).then_inc(cast, 1)
            dve.wait_ge(cast, 2)
            nc.vector.tensor_reduce(lohi[:, 0, :], raw_f[:, 1], AX.X, ALU.min)
            nc.vector.tensor_reduce(lohi[:, 1, :], raw_f[:, 1], AX.X, ALU.max).then_inc(ranged, 1)
            dve.wait_ge(range_done, 1)
            nc.vector.tensor_reduce(lohi_t[:, 0, :], tr[:, 0, :].rearrange("c (g t) -> c g t", t=GT), AX.X, ALU.min)
            nc.vector.tensor_reduce(lohi_t[:, 1, :], tr[:, 1, :].rearrange("c (g t) -> c g t", t=GT), AX.X,
                                    ALU.max).then_inc(range_turned, 1)
            step(nc.vector.memset(ones[:, :], 1.0))
            dve.wait_ge(range_in, 16)
            step(nc.vector.tensor_copy(rng_i[:, :, :], rng[:, :, :]))
            step(nc.vector.tensor_single_scalar(rng_i[:, :, :], rng_i[:, :, :], 7, ALU.arith_shift_right))
            step(nc.vector.tensor_copy(win[:, :, :], rng_i[:, :, :]))
            step(nc.vector.scalar_tensor_tensor(win[:, 1, :], win[:, 1, :], 1.0, win[:, 0, :], ALU.add, ALU.subtract))
            step(nc.vector.tensor_tensor_scan(passes[:, :], ones[:, :], win[:, 1, :], 0.0, ALU.mult, ALU.add))
            nc.vector.tensor_copy(tab_f[:, :, 0], win[:, 0, 0:GROUPS])
            nc.vector.tensor_copy(tab_f[:, :, 1], win[:, 1, 0:GROUPS])
            nc.vector.tensor_copy(tab_f[:, :, 3], win[:, 1, 0:GROUPS])
            step(nc.vector.tensor_tensor(tab_f[:, :, 2], passes[:, 0:GROUPS], win[:, 1, 0:GROUPS], ALU.subtract))
            step(nc.vector.tensor_copy(tab[:, :, :], tab_f[:, :, :]))

        @block.tensor
        def _(pe):
            pe.wait_ge(ranged, 1)
            for k in range(2):
                last = nc.tensor.transpose(tr[:, k, :], lohi[:, k, :], c["ident"][:, :])
            last.then_inc(range_done, 1)
            for n, (k, ch, m) in enumerate(lots):
                if n >= 2:
                    pe.wait_ge(copied, n - 1)
                for i in range(m):
                    rows = min(P, ET - (ch + i) * P)
                    of = raw_w[0:rows, ch + i, :] if k == 2 else raw_f[0:rows, k, ch + i, :]
                    last = nc.tensor.transpose(tp[n % 2][:, i, 0:rows], of, c["ident"][0:rows, 0:rows])
                last.then_inc(turned, 1)

        @block.scalar
        def _(act):
            for n, (k, ch, m) in enumerate(lots):
                act.wait_ge(turned, n + 1)
                cols = min(m * P, ET - ch * P)
                to = (srcf, dstf, wv)[k]
                nc.scalar.copy(to[:, ch * P:ch * P + cols],
                               tp[n % 2].rearrange("p a b -> p (a b)")[:, 0:cols]).then_inc(copied, 1)


def degrees(nc, c, srcf, dstf, wv, deg, table, degin_dram, degin_bc):
    with Scope(nc, "deg") as s:
        node_i = s.sb("node_i", [P, ET], i32)
        part_i = s.sb("part_i", [P, ET], i32)
        lo = s.sb("lo", [P, 2, ET], bf16)
        hi = s.sb("hi", [P, 2, ET], bf16)
        wp = s.sb("wp", [P, 3, ET], bf16)
        rest = s.sb("rest", [P, ET])
        lo_hot = s.sb("lo_hot", [P, 2, GT, P], bf16)
        hi_hot = s.sb("hi_hot", [P, 2, GT, NT], bf16)
        w_hot = s.sb("w_hot", [P, 2, GT, 3, NT], bf16)
        zero = s.sb("zero", [P, 3 * NT], bf16)
        part = s.sb("part", [P, 2, NT])
        out_col = s.sb("out_col", [P, NP, 4])
        acc = [s.ps(f"acc{k}", [P, 3, NT]) for k in range(2)]
        steps, cleared, hi_ready = s.sem("steps"), s.sem("cleared"), s.sem("hi_ready")
        hot_ready = [s.sem(f"hot_ready{k}") for k in range(2)]
        hot_used = [s.sem(f"hot_used{k}") for k in range(2)]
        summed, degree_ready, table_out, dram_out, spread = (
            s.sem("summed"), s.sem("degree_ready"), s.sem("table_out"), s.sem("dram_out"), s.sem("spread"))
        block = s.block()

        @block.vector
        def _(dve):
            step = Steps(dve, steps)
            nc.vector.memset(zero[:, :], 0.0).then_inc(cleared, 1)
            nc.vector.memset(out_col[:, :, :], 0.0)
            for k, node in enumerate((srcf, dstf)):
                step(nc.vector.tensor_copy(node_i[:, :], node[:, 0:ET]))
                step(nc.vector.tensor_single_scalar(part_i[:, :], node_i[:, :], 7, ALU.arith_shift_right))
                step(nc.vector.tensor_copy(hi[:, k, :], part_i[:, :]))
                step(nc.vector.tensor_single_scalar(part_i[:, :], node_i[:, :], P - 1, ALU.bitwise_and))
                step(nc.vector.tensor_copy(lo[:, k, :], part_i[:, :]))
            step(nc.vector.tensor_copy(wp[:, 0, :], wv[:, :]))
            step(nc.vector.tensor_tensor(rest[:, :], wv[:, :], wp[:, 0, :], ALU.subtract))
            step(nc.vector.tensor_copy(wp[:, 1, :], rest[:, :]))
            step(nc.vector.tensor_tensor(rest[:, :], rest[:, :], wp[:, 1, :], ALU.subtract))
            step(nc.vector.tensor_copy(wp[:, 2, :], rest[:, :]))
            with dve.Fori(0, GROUPS) as g:
                for k in range(2):
                    dve.wait_ge(hot_used[k], g)
                    nc.vector.tensor_tensor(hi_hot[:, k], c["iota_bf"][:, 0:NT].unsqueeze(1).to_broadcast([P, GT, NT]),
                                            hi[:, k, ds(g * GT, GT)].unsqueeze(2).to_broadcast([P, GT, NT]),
                                            ALU.is_equal).then_inc(hi_ready, 1)
                    nc.vector.tensor_tensor(lo_hot[:, k], c["iota_bf"][:, :].unsqueeze(1).to_broadcast([P, GT, P]),
                                            lo[:, k, ds(g * GT, GT)].unsqueeze(2).to_broadcast([P, GT, P]), ALU.is_equal)
                    dve.wait_ge(hi_ready, g * 2 + (k + 1))
                    for q in range(3):
                        last = nc.vector.tensor_tensor(w_hot[:, k, :, q, :], hi_hot[:, k],
                                                       wp[:, q, ds(g * GT, GT)].unsqueeze(2).to_broadcast([P, GT, NT]),
                                                       ALU.mult)
                    last.then_inc(hot_ready[k], 1)
            dve.wait_ge(summed, 1)
            for k in range(2):
                step(nc.vector.tensor_copy(part[:, k, :], acc[k][:, 2, :]))
                step(nc.vector.tensor_tensor(part[:, k, :], part[:, k, :], acc[k][:, 1, :], ALU.add))
                step(nc.vector.tensor_tensor(deg[:, k, :], part[:, k, :], acc[k][:, 0, :], ALU.add))
            nc.vector.tensor_copy(out_col[:, 0:NT, 0], deg[:, 0, :]).then_inc(degree_ready, 1)

        @block.tensor
        def _(pe):
            pe.wait_ge(cleared, 1)
            for k in range(2):
                nc.tensor.matmul(acc[k].rearrange("p a b -> p (a b)"), zero[:, 0:P], zero[:, :], start=True, stop=False,
                                 skip_group_check=True)
            with pe.Fori(0, GROUPS) as g:
                for k in range(2):
                    pe.wait_ge(hot_ready[k], g + 1)
                    for j in range(GT):
                        last = nc.tensor.matmul(acc[k].rearrange("p a b -> p (a b)"), lo_hot[:, k, j, :],
                                                w_hot[:, k, j].rearrange("p a b -> p (a b)"), start=False, stop=False,
                                                skip_group_check=True)
                    last.then_inc(hot_used[k], 1)
            for k in range(2):
                last = nc.tensor.matmul(acc[k].rearrange("p a b -> p (a b)"), zero[:, 0:P], zero[:, :], start=False,
                                        stop=True, skip_group_check=True)
            last.then_inc(summed, 1)

        @block.sync
        def _(sp):
            sp.wait_ge(degree_ready, 1)
            sp.dma_start(degin_dram.rearrange("(h l) -> l h", l=P), deg[:, 1, :],
                         allow_slow_non_contiguous=True).then_inc(dram_out, 16)
            sp.dma_start(table[:, D:ROW].rearrange("(h l) c -> l h c", l=P), out_col[:, :, :]).then_inc(table_out, 16)
            sp.wait_ge(dram_out, 16)
            sp.dma_start(degin_bc[:, :], degin_dram.partition_broadcast(P)).then_inc(spread, 16)
            sp.wait_ge(spread, 16)
            sp.wait_ge(table_out, 16)


def layer_norm_scales(step, nc, c, stats, mean, rstd, tmp, wait_sqrt, signal_var):
    step(nc.vector.tensor_tensor(mean, stats[:, :, 1], stats[:, :, 4], ALU.add))
    step(nc.vector.tensor_tensor(tmp, stats[:, :, 1], stats[:, :, 4], ALU.subtract))
    step(nc.vector.tensor_single_scalar(mean, mean, 0.5, ALU.mult))
    step(nc.vector.tensor_tensor(tmp, tmp, tmp, ALU.mult))
    step(nc.vector.tensor_tensor(rstd, stats[:, :, 2], stats[:, :, 5], ALU.add))
    step(nc.vector.tensor_single_scalar(tmp, tmp, 0.25, ALU.mult))
    nc.vector.scalar_tensor_tensor(tmp, rstd, 1.0 / D, tmp, ALU.mult, ALU.add).then_inc(signal_var, 1)
    wait_sqrt()
    step(nc.vector.reciprocal(rstd, tmp))


def load_normalize(nc, c, x, agg):
    with Scope(nc, "ln0") as s:
        stats = s.sb("stats", [P, NP, 6])
        mean, rstd, tmp = s.sb("mean", [P, NP]), s.sb("rstd", [P, NP]), s.sb("tmp", [P, NP])
        padded, loaded, steps = s.sem("padded"), s.sem("loaded"), s.sem("steps")
        gathered, variance, root = s.sem("stats_ready"), s.sem("variance"), s.sem("root")
        block = s.block()

        @block.gpsimd
        def _(pool):
            pool.memset(agg[:, NT - 1:NP, :], 0.0).then_inc(padded, 1)

        @block.sync
        def _(sp):
            sp.dma_start(agg[:, 0:NT - 1, :], x[0:(NT - 1) * P, :].rearrange("(t p) d -> p t d", p=P)).then_inc(loaded, 16)
            sp.wait_ge(padded, 1)
            sp.dma_start(agg[0:LAST, NT - 1, :], x[(NT - 1) * P:NODES, :]).then_inc(loaded, 16)

        @block.vector
        def _(dve):
            step = Steps(dve, steps)
            dve.wait_ge(loaded, 32)
            with dve.Fori(0, NP) as t:
                nc.vector.bn_stats(stats[:, ds(t, 1), :].rearrange("p a b -> p (a b)"),
                                   agg[:, ds(t, 1), :].rearrange("p a b -> p (a b)")).then_inc(gathered, 1)
            dve.wait_ge(gathered, NP)
            layer_norm_scales(step, nc, c, stats, mean[:, :], rstd[:, :], tmp[:, :], lambda: dve.wait_ge(root, 1), variance)
            with dve.Fori(0, NP) as t:
                tile = agg[:, ds(t, 1), :].rearrange("p a b -> p (a b)")
                nc.vector.tensor_scalar(tile, tile, mean[:, ds(t, 1)], rstd[:, ds(t, 1)], ALU.subtract, ALU.mult)

        @block.scalar
        def _(act):
            act.wait_ge(variance, 1)
            nc.scalar.activation(tmp[:, :], tmp[:, :], ACT.Sqrt, bias=c["eps_ln"][:, :]).then_inc(root, 1)


def project(nc, c, name, agg, w, n, func, in_bias, bias_row, finish, extra_sync=None, out_dram=None, stage=None):
    with Scope(nc, name) as s:
        cols = n if out_dram is None else D
        tile_in = [s.sb(f"tile_in{i}", [P, D]) for i in range(2)]
        turn = [s.sb(f"turn{i}", [P, KD, P]) for i in range(2)]
        out = [s.sb(f"out{i}", [P, n]) for i in range(2)]
        tp = [s.ps(f"tp{i}", [P, KD, P]) for i in range(2)]
        mp = [s.ps(f"mp{i}", [P, n]) for i in range(2)]
        turned, copied = [s.sem(f"turned{i}") for i in range(2)], [s.sem(f"copied{i}") for i in range(2)]
        multiplied, finished = [s.sem(f"multiplied{i}") for i in range(2)], [s.sem(f"finished{i}") for i in range(2)]
        stored, loaded = [s.sem(f"stored{i}") for i in range(2)], [s.sem(f"loaded{i}") for i in range(2)]
        xin = [s.sb(f"xin{i}", [P, D]) for i in range(2)] if extra_sync is not None else None
        inner = [s.sem(f"inner{i}") for i in range(2)]
        staged = [s.sem(f"staged{i}") for i in range(2)]
        block = s.block()

        @block.tensor
        def _(pe):
            with pe.Fori(0, NP // 2) as q:
                for i in range(2):
                    pe.wait_ge(copied[i], q)
                    pe.wait_ge(staged[i], q + 1)
                    for k in range(KD):
                        last = nc.tensor.transpose(tp[i][:, k, :], tile_in[i][:, k * P:(k + 1) * P], c["ident"][:, :])
                    last.then_inc(turned[i], 1)
                for i in range(2):
                    pe.wait_ge(copied[i], q + 1)
                    pe.wait_ge(finished[i], q)
                    for k in range(KD):
                        last = nc.tensor.matmul(mp[i][:, :], turn[i][:, k, :], w[:, k, :], start=k == 0,
                                                stop=k == KD - 1 and bias_row is None)
                    if bias_row is not None:
                        last = nc.tensor.matmul(mp[i][:, :], c["ones"][0:1, :], bias_row, start=False, stop=True)
                    last.then_inc(multiplied[i], 1)

        @block.scalar
        def _(act):
            with act.Fori(0, NP // 2) as q:
                for i in range(2):
                    act.wait_ge(turned[i], q + 1)
                    act.wait_ge(multiplied[i], q)
                    if in_bias is None:
                        nc.scalar.activation(turn[i][:, :, :], tp[i][:, :, :], func).then_inc(copied[i], 1)
                    else:
                        for k in range(KD):
                            last = nc.scalar.activation(turn[i][:, k, :], tp[i][:, k, :], func, bias=in_bias[:, k:k + 1])
                        last.then_inc(copied[i], 1)

        @block.vector
        def _(dve):
            with dve.Fori(0, NP // 2) as q:
                for i in range(2):
                    dve.wait_ge(turned[i], q)
                    nc.vector.tensor_copy(tile_in[i][:, :], agg[:, ds(q * 2 + i, 1), :].rearrange("p a b -> p (a b)")
                                          ).then_inc(staged[i], 1)
                for i in range(2):
                    dve.wait_ge(multiplied[i], q + 1)
                    if extra_sync is not None:
                        dve.wait_ge(loaded[i], q * 16 + 16)
                    if out_dram is not None:
                        dve.wait_ge(stored[i], q * 16)
                    finish(dve, q * 2 + i, q, i, mp[i], out[i], xin[i] if xin else None, inner[i], finished[i])

        @block.sync
        def _(sp):
            if out_dram is not None or extra_sync is not None:
                with sp.Fori(0, NP // 2) as q:
                    for i in range(2):
                        if extra_sync is not None:
                            sp.wait_ge(finished[i], q)
                            sp.dma_start(xin[i][:, :], extra_sync[ds((q * 2 + i) * P, P), :]).then_inc(loaded[i], 16)
                    for i in range(2):
                        if out_dram is not None:
                            sp.wait_ge(finished[i], q + 1)
                            to, of = out_dram(q * 2 + i, out[i])
                            sp.dma_start(to, of).then_inc(stored[i], 16)
                if out_dram is not None:
                    for i in range(2):
                        sp.wait_ge(stored[i], NP // 2 * 16)


def aggregate(nc, c, name, table, srcf, dstf, wv, degin_bc, tab, agg):
    with Scope(nc, name) as s:
        idx = s.sb("idx", [P, SLOTS, GT], u32)
        rows = s.sb("rows", [P, SLOTS, GT, ROW])
        hot = s.sb("hot", [P, GT, P])
        near = s.sb("near", [P, GT])
        di = s.sb("di", [P, GT])
        dd = s.sb("dd", [P, GT])
        root_sb = s.sb("root", [P, GT])
        norm = s.sb("norm", [P, GT])
        acc = s.ps("acc", [P, D])
        cleared, opened = s.sem("cleared"), s.sem("opened")
        staged, gathered = [s.sem(f"staged{i}") for i in range(SLOTS)], [s.sem(f"gathered{i}") for i in range(SLOTS)]
        near_ready, in_degree, product, root, inverse, norm_ready = (
            s.sem("near_ready"), s.sem("in_degree"), s.sem("product"), s.sem("root_ready"), s.sem("inverse"), s.sem("norm_ready"))
        hot_ready, summed, added = s.sem("hot_ready"), s.sem("summed"), s.sem("added")
        block = s.block()

        @block.gpsimd
        def _(pool):
            with pool.Fori(0, GROUPS // SLOTS) as q:
                for i in range(SLOTS):
                    pool.wait_ge(staged[i], q + 1)
                    pool.sem_inc(opened, 1)
                    for j in range(GT):
                        pool.indirect_dma_start(out=rows[:, i, j, :], out_offset=None, in_=table[:, :],
                                                in_offset=bass.IndirectOffsetOnAxis(ap=idx[:, i, j:j + 1], axis=0)
                                                ).then_inc(gathered[i], 16)
            for i in range(SLOTS):
                pool.wait_ge(gathered[i], GROUPS // SLOTS * GT * 16)

        @block.scalar
        def _(act):
            for i in range(SLOTS):
                nc.scalar.copy(idx[:, i, :], srcf[:, i * GT:(i + 1) * GT]).then_inc(staged[i], 1)
            with act.Fori(0, GROUPS // SLOTS) as q:
                for i in range(SLOTS):
                    g = q * SLOTS + i
                    spans = act.value_load(tab[0:1, ds(g, 1), 1:2].rearrange("a b c -> a (b c)"), min_val=1, max_val=NP)
                    before = act.value_load(tab[0:1, ds(g, 1), 2:3].rearrange("a b c -> a (b c)"), min_val=0, max_val=GROUPS * NP)
                    with act.Fori(0, spans) as n:
                        act.wait_ge(product, before + n + 1)
                        nc.scalar.activation(root_sb[:, :], dd[:, :], ACT.Sqrt, bias=c["eps_gcn"][:, :]).then_inc(root, 1)
                    act.wait_ge(summed, before + spans)
                    nc.scalar.copy(idx[:, i, :], srcf[:, ds((g + SLOTS) * GT, GT)]).then_inc(staged[i], 1)

        @block.vector
        def _(dve):
            nc.vector.memset(agg[:, :, :], 0.0).then_inc(cleared, 1)
            dve.wait_ge(cleared, 1)
            with dve.Fori(0, GROUPS // SLOTS) as q:
                for i in range(SLOTS):
                    g = q * SLOTS + i
                    first = dve.value_load(tab[0:1, ds(g, 1), 0:1].rearrange("a b c -> a (b c)"), min_val=0, max_val=NT - 1)
                    spans = dve.value_load(tab[0:1, ds(g, 1), 1:2].rearrange("a b c -> a (b c)"), min_val=1, max_val=NT)
                    before = dve.value_load(tab[0:1, ds(g, 1), 2:3].rearrange("a b c -> a (b c)"), min_val=0, max_val=GROUPS * NP)
                    with dve.Fori(0, spans) as n:
                        w = nc.s_assert_within(first + n, 0, NT - 1,
                                                 skip_runtime_bounds_check_because="it ends at the last target's window")
                        p1 = before + n + 1
                        nc.vector.tensor_scalar(near[:, :], dstf[:, ds(g * GT, GT)], c["window"][:, ds(w, 1)], None,
                                                ALU.subtract).then_inc(near_ready, 1)
                        dve.wait_ge(near_ready, p1)
                        for j in range(GT):
                            last = nc.vector.scalar_tensor_tensor(hot[:, j, :], c["iota"][:, :], near[:, j:j + 1],
                                                                  degin_bc[:, ds(w * P, P)], ALU.is_equal, ALU.mult,
                                                                  accum_out=di[:, j:j + 1])
                        last.then_inc(in_degree, 1)
                        dve.wait_ge(in_degree, p1)
                        dve.wait_ge(gathered[i], q * (GT * 16) + GT * 16)
                        nc.vector.tensor_tensor(dd[:, :], rows[:, i, :, D], di[:, :], ALU.mult).then_inc(product, 1)
                        dve.wait_ge(root, p1)
                        nc.vector.reciprocal(norm[:, :], root_sb[:, :]).then_inc(inverse, 1)
                        dve.wait_ge(inverse, p1)
                        nc.vector.tensor_tensor(norm[:, :], norm[:, :], wv[:, ds(g * GT, GT)], ALU.mult).then_inc(norm_ready, 1)
                        dve.wait_ge(norm_ready, p1)
                        for j in range(GT):
                            nc.vector.tensor_scalar(hot[:, j, :], c["iota"][:, :], near[:, j:j + 1], norm[:, j:j + 1],
                                                    ALU.is_equal, ALU.mult).then_inc(hot_ready, 1)
                        dve.wait_ge(summed, p1)
                        to = agg[:, ds(w, 1), :].rearrange("p a b -> p (a b)")
                        nc.vector.tensor_tensor(to, to, acc[:, :], ALU.add).then_inc(added, 1)
                        dve.wait_ge(added, p1)

        @block.tensor
        def _(pe):
            with pe.Fori(0, GROUPS // SLOTS) as q:
                for i in range(SLOTS):
                    g = q * SLOTS + i
                    spans = pe.value_load(tab[0:1, ds(g, 1), 1:2].rearrange("a b c -> a (b c)"), min_val=1, max_val=NP)
                    before = pe.value_load(tab[0:1, ds(g, 1), 2:3].rearrange("a b c -> a (b c)"), min_val=0, max_val=GROUPS * NP)
                    with pe.Fori(0, spans) as n:
                        for j in range(GT):
                            pe.wait_ge(hot_ready, (before + n) * GT + (j + 1))
                            last = nc.tensor.matmul(acc[:, :], hot[:, j, :], rows[:, i, j, 0:D], start=j == 0, stop=j == GT - 1)
                        last.then_inc(summed, 1)


def route(nc, c, logits, agg, g1, g2, pos, expert_of):
    with Scope(nc, "route") as s:
        top = s.sb("top", [P, NP, 8])
        at = s.sb("at", [P, NP, 8], u32)
        atf = s.sb("atf", [P, NP, 2])
        valid = s.sb("valid", [P, NP])
        hot1, hot2, both = s.sb("hot1", [P, NP, E]), s.sb("hot2", [P, NP, E]), s.sb("both", [P, NP, E])
        ex, sm = s.sb("ex", [P, NP]), s.sb("sm", [P, NP])
        total = s.sb("total", [P, E, NP])
        upto = s.sb("upto", [P, E, NP])
        keep = s.sb("keep", [P, E, NP])
        count, count_i = s.sb("count", [P, E]), s.sb("count_i", [P, E], i32)
        tiles, ends, ones = s.sb("tiles", [P, E]), s.sb("ends", [P, E]), s.sb("ones", [P, E])
        place = s.sb("place", [P, NP, E])
        posf = s.sb("posf", [P, NP])
        slot, passed, eof = s.sb("slot", [1, ST]), s.sb("passed", [1, ST, E]), s.sb("eof", [1, ST])
        half = NP // 2
        rank = [s.ps(f"rank{i}", [P, half, E]) for i in range(2)]
        tot = [s.ps(f"tot{i}", [P, half, E]) for i in range(2)]
        steps, diff, expd, chosen, ranked, slots = (
            s.sem("steps"), s.sem("diff"), s.sem("expd"), s.sem("chosen"), s.sem("ranked"), s.sem("slots"))
        topped = s.sem("topped")
        block = s.block()

        @block.gpsimd
        def _(pool):
            pool.iota(slot[:, :], pattern=[[1, ST]], base=0, channel_multiplier=0,
                      allow_small_or_imprecise_dtypes=True)
            pool.memset(keep[:, :, :], 1.0).then_inc(slots, 1)
            pool.wait_ge(slots, 1)
            pool.memset(keep[:, :, 0:1], 0.0).then_inc(slots, 1)

        @block.vector
        def _(dve):
            step = Steps(dve, steps)
            for t in range(NP):
                last = nc.vector.max(top[:, t, :], logits[:, t, :])
            last.then_inc(topped, 1)
            dve.wait_ge(topped, 1)
            for t in range(NP):
                last = nc.vector.max_index(at[:, t, :], top[:, t, :], logits[:, t, :])
            step(last)
            step(nc.vector.tensor_tensor(ex[:, :], top[:, :, 1], top[:, :, 0], ALU.subtract))
            nc.vector.tensor_copy(posf[:, :], ex[:, :]).then_inc(diff, 1)
            step(nc.vector.tensor_copy(atf[:, :, :], at[:, :, 0:2]))
            step(nc.vector.tensor_single_scalar(valid[:, :], c["token"][:, :], float(NODES), ALU.is_lt))
            for k, h in enumerate((hot1, hot2)):
                step(nc.vector.tensor_tensor(h[:, :, :], c["iota"][:, 0:E].unsqueeze(1).to_broadcast([P, NP, E]),
                                             atf[:, :, k:k + 1].to_broadcast([P, NP, E]), ALU.is_equal))
                step(nc.vector.tensor_tensor(h[:, :, :], h[:, :, :], valid[:, :].unsqueeze(2).to_broadcast([P, NP, E]),
                                             ALU.mult))
            nc.vector.tensor_tensor(both[:, :, :], hot1[:, :, :], hot2[:, :, :], ALU.add).then_inc(chosen, 1)
            dve.wait_ge(expd, 1)
            step(nc.vector.tensor_single_scalar(sm[:, :], ex[:, :], 1.0, ALU.add))
            step(nc.vector.reciprocal(g1[:, :], sm[:, :]))
            step(nc.vector.tensor_tensor(g2[:, :], ex[:, :], g1[:, :], ALU.mult))
            dve.wait_ge(ranked, 1)
            dve.wait_ge(slots, 2)
            for i in range(2):
                last = nc.vector.tensor_copy(total[:, :, i * half:(i + 1) * half], tot[i][:, :, :].rearrange("p t e -> p e t"))
            step(last)
            step(nc.vector.tensor_tensor_scan(upto.rearrange("p e t -> p (e t)"), keep.rearrange("p e t -> p (e t)"),
                                              total.rearrange("p e t -> p (e t)"), 0.0, ALU.mult, ALU.add))
            step(nc.vector.tensor_single_scalar(count[:, :], upto[:, :, NP - 1], float(P - 1), ALU.add))
            step(nc.vector.tensor_copy(count_i[:, :], count[:, :]))
            step(nc.vector.tensor_single_scalar(count_i[:, :], count_i[:, :], 7, ALU.arith_shift_right))
            step(nc.vector.tensor_copy(tiles[:, :], count_i[:, :]))
            step(nc.vector.memset(ones[:, :], 1.0))
            step(nc.vector.tensor_tensor_scan(ends[:, :], ones[:, :], tiles[:, :], 0.0, ALU.mult, ALU.add))
            step(nc.vector.tensor_tensor(passed[:, :, :], ends[0:1, :].unsqueeze(1).to_broadcast([1, ST, E]),
                                         slot[:, :].unsqueeze(2).to_broadcast([1, ST, E]), ALU.is_le))
            step(nc.vector.tensor_reduce(eof[:, :], passed[:, :, :], AX.X, ALU.add))
            step(nc.vector.tensor_single_scalar(eof[:, :], eof[:, :], float(E - 1), ALU.min))
            step(nc.vector.tensor_copy(expert_of[:, :], eof[:, :]))
            step(nc.vector.tensor_tensor(tiles[:, :], ends[:, :], tiles[:, :], ALU.subtract))
            step(nc.vector.tensor_single_scalar(tiles[:, :], tiles[:, :], float(P), ALU.mult))
            step(nc.vector.tensor_tensor(upto[:, :, :], upto[:, :, :], total[:, :, :], ALU.subtract))
            step(nc.vector.tensor_tensor(upto[:, :, :], upto[:, :, :], tiles[:, :].unsqueeze(2).to_broadcast([P, E, NP]), ALU.add))
            for i in range(2):
                last = nc.vector.tensor_tensor(place[:, i * half:(i + 1) * half, :], rank[i][:, :, :],
                                               upto[:, :, i * half:(i + 1) * half].rearrange("p e t -> p t e"), ALU.add)
            step(last)
            for k, h in enumerate((hot1, hot2)):
                step(nc.vector.tensor_tensor(h[:, :, :], h[:, :, :], place[:, :, :], ALU.mult))
                step(nc.vector.tensor_reduce(posf[:, :], h[:, :, :], AX.X, ALU.add))
                step(nc.vector.tensor_copy(pos[:, k, :], posf[:, :]))

        @block.scalar
        def _(act):
            act.wait_ge(diff, 1)
            nc.scalar.activation(ex[:, :], ex[:, :], ACT.Exp).then_inc(expd, 1)

        @block.tensor
        def _(pe):
            pe.wait_ge(chosen, 1)
            for i in range(2):
                of = both[:, i * half:(i + 1) * half, :].rearrange("p t e -> p (t e)")
                nc.tensor.matmul(rank[i].rearrange("p t e -> p (t e)"), c["tri"][:, :], of, start=True, stop=True)
                last = nc.tensor.matmul(tot[i].rearrange("p t e -> p (t e)"), c["ones"][:, :], of, start=True, stop=True)
            last.then_inc(ranked, 1)


def clear_slots(nc, slots_dram):
    with Scope(nc, "clear") as s:
        zero = s.sb("zero", [P, 6 * D])
        filled, done = s.sem("filled"), s.sem("done")
        block = s.block()

        @block.vector
        def _(dve):
            nc.vector.memset(zero[:, :], 0.0).then_inc(filled, 1)

        @block.sync
        def _(sp):
            sp.wait_ge(filled, 1)
            for t in range(0, ST, 6):
                sp.dma_start(slots_dram[t * P:(t + 6) * P, :].rearrange("(p r) d -> p (r d)", p=P), zero[:, :]).then_inc(done, 16)
            sp.wait_ge(done, 16 * (ST // 6))


def scatter(nc, agg, pos, slots_dram):
    with Scope(nc, "scatter") as s:
        sent = s.sem("sent")
        block = s.block()

        @block.gpsimd
        def _(pool):
            for t in range(NT):
                n = P if t < NT - 1 else LAST
                for k in range(2):
                    pool.indirect_dma_start(out=slots_dram[:, :],
                                            out_offset=bass.IndirectOffsetOnAxis(ap=pos[0:n, k, t:t + 1], axis=0),
                                            in_=agg[0:n, t, :], in_offset=None).then_inc(sent, 16)
            pool.wait_ge(sent, 16 * 2 * NT)


def experts(nc, c, w1, b1, w2, b2, slots_dram, moe_dram, expert_of):
    with Scope(nc, "ffn") as s:
        w1_sb = s.sb("w1", [P, E * KD * F])
        w2_sb = s.sb("w2", [P, E * FC * D])
        b1_row = s.sb("b1_row", [E * FC, P])
        b1_sb = s.sb("b1", [P, E * FC])
        b2_sb = [s.sb(f"b2{i}", [P, D]) for i in range(2)]
        xs = [s.sb(f"xs{i}", [P, D]) for i in range(2)]
        xt = [s.sb(f"xt{i}", [P, KD, P]) for i in range(2)]
        hs = [s.sb(f"hs{i}", [P, F]) for i in range(2)]
        ht = [s.sb(f"ht{i}", [P, FC, P]) for i in range(2)]
        ys = [s.sb(f"ys{i}", [P, D]) for i in range(2)]
        tp = [s.ps(f"tp{i}", [P, KD, P]) for i in range(2)]
        hp = [s.ps(f"hp{i}", [P, F]) for i in range(2)]
        htp = [s.ps(f"htp{i}", [P, FC, P]) for i in range(2)]
        yp = [s.ps(f"yp{i}", [P, D]) for i in range(2)]
        bp = htp[0][:, 0, 0:E * FC]
        two = range(2)
        weights, biased, bias_turned = s.sem("weights"), s.sem("biased"), s.sem("bias_turned")
        loaded, turned, copied, up, taken, hidden_turned, rectified, down, out_ready, stored, biases = (
            [s.sem(f"{x}{i}") for i in two]
            for x in ("loaded", "turned", "copied", "up", "taken", "hidden_turned", "rectified", "down", "out_ready",
                      "stored", "biases"))
        block = s.block()

        @block.sync
        def _(sp):
            sp.dma_start(b1_row[:, :], b1.rearrange("e (c p) -> (e c) p", p=P)).then_inc(weights, 16)
            sp.dma_start(w1_sb[:, :].rearrange("p (e k f) -> p e k f", e=E, k=KD),
                         w1.rearrange("e (k p) f -> p e k f", p=P)).then_inc(weights, 16)
            sp.dma_start(w2_sb[:, :].rearrange("p (e c d) -> p e c d", e=E, c=FC),
                         w2.rearrange("e (c p) d -> p e c d", p=P)).then_inc(weights, 16)
            with sp.Fori(0, ST // 2) as q:
                for i in two:
                    sp.wait_ge(turned[i], q)
                    sp.dma_start(xs[i][:, :], slots_dram[ds((q * 2 + i) * P, P), :]).then_inc(loaded[i], 16)
                e = [sp.value_load(expert_of[0:1, ds(q * 2 + i, 1)], min_val=0, max_val=E - 1) for i in two]
                for i in two:
                    sp.wait_ge(out_ready[i], q)
                    sp.dma_start(b2_sb[i][:, :], b2[ds(e[i], 1), :].rearrange("a d -> (a d)").partition_broadcast(P)
                                 ).then_inc(biases[i], 16)

        @block.gpsimd
        def _(pool):
            with pool.Fori(0, ST // 2) as q:
                for i in two:
                    pool.wait_ge(out_ready[i], q + 1)
                    pool.dma_start(moe_dram[ds((q * 2 + i) * P, P), :], ys[i][:, :]).then_inc(stored[i], 16)
            for i in two:
                pool.wait_ge(stored[i], ST // 2 * 16)

        @block.tensor
        def _(pe):
            pe.wait_ge(weights, 48)
            nc.tensor.transpose(bp, b1_row[:, :], c["ident"][0:E * FC, 0:E * FC]).then_inc(bias_turned, 1)
            pe.wait_ge(biased, 1)
            with pe.Fori(0, ST // 2) as q:
                for i in two:
                    pe.wait_ge(loaded[i], q * 16 + 16)
                    pe.wait_ge(copied[i], q)
                    for k in range(KD):
                        last = nc.tensor.transpose(tp[i][:, k, :], xs[i][:, k * P:(k + 1) * P], c["ident"][:, :])
                    last.then_inc(turned[i], 1)
                e = [pe.value_load(expert_of[0:1, ds(q * 2 + i, 1)], min_val=0, max_val=E - 1) for i in two]
                for i in two:
                    pe.wait_ge(copied[i], q + 1)
                    pe.wait_ge(taken[i], q)
                    for k in range(KD):
                        last = nc.tensor.matmul(hp[i][:, :], xt[i][:, k, :], w1_sb[:, ds(e[i] * (KD * F) + k * F, F)],
                                                start=k == 0, stop=k == KD - 1)
                    last.then_inc(up[i], 1)
                for i in two:
                    pe.wait_ge(taken[i], q + 1)
                    pe.wait_ge(rectified[i], q)
                    for f in range(FC):
                        last = nc.tensor.transpose(htp[i][:, f, :], hs[i][:, f * P:(f + 1) * P], c["ident"][:, :])
                    last.then_inc(hidden_turned[i], 1)
                for i in two:
                    pe.wait_ge(rectified[i], q + 1)
                    pe.wait_ge(out_ready[i], q)
                    for f in range(FC):
                        last = nc.tensor.matmul(yp[i][:, :], ht[i][:, f, :], w2_sb[:, ds(e[i] * (FC * D) + f * D, D)],
                                                start=f == 0, stop=f == FC - 1)
                    last.then_inc(down[i], 1)

        @block.scalar
        def _(act):
            act.wait_ge(bias_turned, 1)
            nc.scalar.copy(b1_sb[:, :], bp).then_inc(biased, 1)
            act.wait_ge(biased, 1)
            with act.Fori(0, ST // 2) as q:
                e = [act.value_load(expert_of[0:1, ds(q * 2 + i, 1)], min_val=0, max_val=E - 1) for i in two]
                for i in two:
                    act.wait_ge(hidden_turned[i], q + 1)
                    act.wait_ge(down[i], q)
                    for f in range(FC):
                        last = nc.scalar.activation(ht[i][:, f, :], htp[i][:, f, :], ACT.Relu,
                                                    bias=b1_sb[:, ds(e[i] * FC + f, 1)])
                    last.then_inc(rectified[i], 1)

        @block.vector
        def _(dve):
            with dve.Fori(0, ST // 2) as q:
                for i in two:
                    dve.wait_ge(turned[i], q + 1)
                    dve.wait_ge(up[i], q)
                    nc.vector.tensor_copy(xt[i][:, :, :], tp[i][:, :, :]).then_inc(copied[i], 1)
                for i in two:
                    dve.wait_ge(up[i], q + 1)
                    dve.wait_ge(hidden_turned[i], q)
                    nc.vector.tensor_copy(hs[i][:, :], hp[i][:, :]).then_inc(taken[i], 1)
                for i in two:
                    dve.wait_ge(down[i], q + 1)
                    dve.wait_ge(biases[i], q * 16 + 16)
                    dve.wait_ge(stored[i], q * 16)
                    nc.vector.tensor_tensor(ys[i][:, :], yp[i][:, :], b2_sb[i][:, :], ALU.add).then_inc(out_ready[i], 1)


def combine(nc, c, agg, g1, g2, pos, moe_dram, x1_dram, gamma, beta, out):
    with Scope(nc, "comb") as s:
        NB = 4
        rows = [s.sb(f"rows{i}", [P, 2, D]) for i in range(NB)]
        gb = s.sb("gb", [P, 2, D])
        x1 = [s.sb(f"x1{i}", [P, D]) for i in range(2)]
        res = [s.sb(f"res{i}", [P, D]) for i in range(2)]
        stats = s.sb("stats", [P, NP, 6])
        mean, rstd, tmp = s.sb("mean", [P, NP]), s.sb("rstd", [P, NP]), s.sb("tmp", [P, NP])
        fetched = [s.sem(f"fetched{i}") for i in range(NB)]
        steps, used, first_in, y_ready, measured = (
            s.sem("steps"), s.sem("used"), s.sem("first_in"), s.sem("y_ready"), s.sem("measured"))
        variance, root, params = s.sem("variance"), s.sem("root"), s.sem("params")
        got = [s.sem(f"got{i}") for i in range(2)]
        n1, n2, n3, ready, stored = ([s.sem(f"{x}{i}") for i in range(2)] for x in ("n1", "n2", "n3", "ready", "stored"))
        block = s.block()

        @block.gpsimd
        def _(pool):
            for t in range(NT):
                n = P if t < NT - 1 else LAST
                if t >= NB:
                    pool.wait_ge(used, t - NB + 1)
                for k in range(2):
                    pool.indirect_dma_start(out=rows[t % NB][0:n, k, :], out_offset=None, in_=moe_dram[:, :],
                                            in_offset=bass.IndirectOffsetOnAxis(ap=pos[0:n, k, t:t + 1], axis=0)
                                            ).then_inc(fetched[t % NB], 16)

        @block.vector
        def _(dve):
            step = Steps(dve, steps)
            for t in range(NT):
                n = P if t < NT - 1 else LAST
                dve.wait_ge(fetched[t % NB], 32 * (t // NB + 1))
                nc.vector.scalar_tensor_tensor(agg[0:n, t, :], rows[t % NB][0:n, 0, :], g1[0:n, t:t + 1], agg[0:n, t, :],
                                               ALU.mult, ALU.add).then_inc(first_in, 1)
                dve.wait_ge(first_in, t + 1)
                nc.vector.scalar_tensor_tensor(agg[0:n, t, :], rows[t % NB][0:n, 1, :], g2[0:n, t:t + 1], agg[0:n, t, :],
                                               ALU.mult, ALU.add).then_inc(used, 1)
                dve.wait_ge(used, t + 1)
                last = nc.vector.bn_stats(stats[:, t, :], agg[:, t, :])
            step(nc.vector.bn_stats(stats[:, NT, :], agg[:, NT, :]))
            layer_norm_scales(step, nc, c, stats, mean[:, :], rstd[:, :], tmp[:, :], lambda: dve.wait_ge(root, 1), variance)
            dve.wait_ge(params, 32)
            with dve.Fori(0, NP // 2) as q:
                for i in range(2):
                    tile = agg[:, ds(q * 2 + i, 1), :].rearrange("p a b -> p (a b)")
                    dve.wait_ge(stored[i], q * 16)
                    nc.vector.tensor_scalar(res[i][:, :], tile, mean[:, ds(q * 2 + i, 1)], rstd[:, ds(q * 2 + i, 1)],
                                            ALU.subtract, ALU.mult).then_inc(n1[i], 1)
                for i in range(2):
                    dve.wait_ge(n1[i], q + 1)
                    nc.vector.tensor_tensor(res[i][:, :], res[i][:, :], gb[:, 0, :], ALU.mult).then_inc(n2[i], 1)
                for i in range(2):
                    dve.wait_ge(n2[i], q + 1)
                    nc.vector.tensor_tensor(res[i][:, :], res[i][:, :], gb[:, 1, :], ALU.add).then_inc(n3[i], 1)
                for i in range(2):
                    dve.wait_ge(n3[i], q + 1)
                    dve.wait_ge(got[i], q * 16 + 16)
                    nc.vector.tensor_tensor(res[i][:, :], res[i][:, :], x1[i][:, :], ALU.add).then_inc(ready[i], 1)

        @block.scalar
        def _(act):
            act.dma_start(gb[:, 0, :], gamma.partition_broadcast(P)).then_inc(params, 16)
            act.dma_start(gb[:, 1, :], beta.partition_broadcast(P)).then_inc(params, 16)
            act.wait_ge(variance, 1)
            nc.scalar.activation(tmp[:, :], tmp[:, :], ACT.Sqrt, bias=c["eps_ln"][:, :]).then_inc(root, 1)
            with act.Fori(0, NP // 2) as q:
                for i in range(2):
                    act.wait_ge(ready[i], q)
                    act.dma_start(x1[i][:, :], x1_dram[ds((q * 2 + i) * P, P), :]).then_inc(got[i], 16)

        @block.sync
        def _(sp):
            with sp.Fori(0, (NT - 1) // 2) as q:
                for i in range(2):
                    sp.wait_ge(ready[i], q + 1)
                    sp.dma_start(out[ds((q * 2 + i) * P, P), :], res[i][:, :]).then_inc(stored[i], 16)
            sp.wait_ge(ready[0], NP // 2)
            sp.dma_start(out[(NT - 1) * P:NODES, :], res[0][0:LAST, :]).then_inc(stored[0], 16)
            sp.wait_ge(stored[0], 16 * (NP // 2))
            sp.wait_ge(stored[1], 16 * (NP // 2 - 1))


def gnn_moe(nc, x, src, dst, edge_weight, W6, b6, W7, b7, Wp, bp, gate_w, gate_b, w1, b1, w2, b2, gamma, beta, out):
    table = [nc.dram_tensor(f"table{i}", [NP * P, ROW], f32).ap() for i in range(2)]
    range_dram = nc.dram_tensor("edge_ranges", [2, EC * (P // GT)], f32).ap()
    degin_dram = nc.dram_tensor("in_degrees", [NT * P], f32).ap()
    x_pad = nc.dram_tensor("x_pad", [NP * P, D], f32).ap()
    x1_dram = nc.dram_tensor("x1", [NP * P, D], f32).ap()
    slots_dram = nc.dram_tensor("slots", [ST * P, D], f32).ap()
    moe_dram = nc.dram_tensor("moe", [ST * P, D], f32).ap()

    with Scope(nc, "all") as top:
        agg = top.sb("agg", [P, NP, D])
        c = {n: top.sb(n, [P, P]) for n in ("ident", "tri", "ones", "iota")}
        c["iota_bf"] = top.sb("iota_bf", [P, P], bf16)
        c["window"], c["token"] = top.sb("window", [P, NP]), top.sb("token", [P, NP])
        c["eps_ln"], c["eps_gcn"] = top.sb("eps_ln", [P, 1]), top.sb("eps_gcn", [P, 1])
        g1, g2 = top.sb("g1", [P, NP]), top.sb("g2", [P, NP])
        pos = top.sb("pos", [P, 2, NP], u32)
        expert_of = top.sb("expert_of", [1, ST], i32)
        constants(nc, c)
        clear_slots(nc, slots_dram)

        with Scope(nc, "gnn") as s:
            w6, w7, wp = (s.sb(n, [P, KD, D]) for n in ("w6", "w7", "wp"))
            b67 = s.sb("b67", [P, 2, KD])
            bpr = s.sb("bp", [1, D])
            degin_bc = s.sb("degin_bc", [P, NT * P])
            srcf, dstf, wv = s.sb("srcf", [P, ET + SLOTS * GT]), s.sb("dstf", [P, ET]), s.sb("wv", [P, ET])
            deg = s.sb("deg", [P, 2, NT])
            tab = s.sb("tab", [1, GROUPS, 4], i32)
            small_loads(nc, (w6, w7, wp, b67, bpr), (W6, W7, Wp, b6, b7, bp), x, x_pad)
            edge_tables(nc, c, src, dst, edge_weight, range_dram, srcf, dstf, wv, tab)
            degrees(nc, c, srcf, dstf, wv, deg, table[0], degin_dram, degin_bc)
            copy_degrees(nc, deg, table[1])
            load_normalize(nc, c, x, agg)

            def copy_out(dve, t, q, i, product, out_sb, _, inner, finished):
                nc.vector.tensor_copy(out_sb[:, :], product[:, :]).then_inc(finished, 1)

            def to_table(which):
                return lambda t, out_sb: (table[which][ds(t * P, P), 0:D], out_sb[:, :])

            project(nc, c, "lin6", agg, w6, D, ACT.Copy, None, None, copy_out, out_dram=to_table(0))
            aggregate(nc, c, "agg6", table[0], srcf, dstf, wv, degin_bc, tab, agg)
            project(nc, c, "lin7", agg, w7, D, ACT.Relu, b67[:, 0, :], None, copy_out, out_dram=to_table(1))
            aggregate(nc, c, "agg7", table[1], srcf, dstf, wv, degin_bc, tab, agg)

            def residual(dve, t, q, i, product, out_sb, xin, inner, finished):
                tile = agg[:, ds(t, 1), :].rearrange("p a b -> p (a b)")
                nc.vector.tensor_tensor(tile, product[:, :], xin[:, :], ALU.add).then_inc(finished, 1)

            project(nc, c, "linp", agg, wp, D, ACT.Relu, b67[:, 1, :], bpr[0:1, :], residual, extra_sync=x_pad,
                    out_dram=lambda t, _: (x1_dram[ds(t * P, P), :], agg[:, ds(t, 1), :].rearrange("p a b -> p (a b)")))

        normalize(nc, c, agg)
        with Scope(nc, "moe") as s:
            logits = s.sb("logits", [P, NP, E])
            gw, gbr = s.sb("gw", [P, KD, E]), s.sb("gbr", [1, E])
            gate_loads(nc, gw, gbr, gate_w, gate_b)

            def keep(dve, t, q, i, product, out_sb, _, inner, finished):
                nc.vector.tensor_copy(logits[:, ds(t, 1), :].rearrange("p a b -> p (a b)"), product[:, :]).then_inc(finished, 1)

            project(nc, c, "gate", agg, gw, E, ACT.Copy, None, gbr[0:1, :], keep)
            route(nc, c, logits, agg, g1, g2, pos, expert_of)
        scatter(nc, agg, pos, slots_dram)
        experts(nc, c, w1, b1, w2, b2, slots_dram, moe_dram, expert_of)
        combine(nc, c, agg, g1, g2, pos, moe_dram, x1_dram, gamma, beta, out)


def small_loads(nc, to, of, x, x_pad):
    w6, w7, wp, b67, bpr = to
    W6, W7, Wp, b6, b7, bp = of
    with Scope(nc, "small") as s:
        loaded = s.sem("loaded")
        zero = s.sb("zero", [P, D])
        zeroed = s.sem("zeroed")
        block = s.block()

        @block.vector
        def _(dve):
            nc.vector.memset(zero[:, :], 0.0).then_inc(zeroed, 1)

        @block.sync
        def _(sp):
            for t, w in ((w6, W6), (w7, W7), (wp, Wp)):
                sp.dma_start(t[:, :, :], w.rearrange("(k p) d -> p k d", p=P)).then_inc(loaded, 16)
            for i, b in enumerate((b6, b7)):
                sp.dma_start(b67[:, i, :], b.rearrange("(k p) -> p k", p=P), allow_slow_non_contiguous=True).then_inc(loaded, 16)
            sp.dma_start(bpr[:, :], bp.rearrange("(a d) -> a d", a=1)).then_inc(loaded, 16)
            sp.dma_start(x_pad[0:NODES, :], x[:, :]).then_inc(loaded, 16)
            sp.wait_ge(zeroed, 1)
            rest = NP * P - NODES
            for a in range(0, rest, P):
                n = min(P, rest - a)
                sp.dma_start(x_pad[NODES + a:NODES + a + n, :], zero[0:n, :]).then_inc(loaded, 16)
            sp.wait_ge(loaded, 16 * (7 + -(-rest // P)))


def gate_loads(nc, gw, gbr, gate_w, gate_b):
    with Scope(nc, "gload") as s:
        loaded = s.sem("loaded")
        block = s.block()

        @block.sync
        def _(sp):
            sp.dma_start(gw[:, :, :], gate_w.rearrange("(k p) e -> p k e", p=P)).then_inc(loaded, 16)
            sp.dma_start(gbr[:, :], gate_b.rearrange("(a e) -> a e", a=1)).then_inc(loaded, 16)
            sp.wait_ge(loaded, 32)


def copy_degrees(nc, deg, table):
    with Scope(nc, "cdeg") as s:
        out_col = s.sb("out_col", [P, NP, 4])
        zeroed, ready, done = s.sem("zeroed"), s.sem("ready"), s.sem("done")
        block = s.block()

        @block.vector
        def _(dve):
            nc.vector.memset(out_col[:, :, :], 0.0).then_inc(zeroed, 1)
            dve.wait_ge(zeroed, 1)
            nc.vector.tensor_copy(out_col[:, 0:NT, 0], deg[:, 0, :]).then_inc(ready, 1)

        @block.sync
        def _(sp):
            sp.wait_ge(ready, 1)
            sp.dma_start(table[:, D:ROW].rearrange("(h l) c -> l h c", l=P), out_col[:, :, :]).then_inc(done, 16)
            sp.wait_ge(done, 16)


def normalize(nc, c, agg):
    with Scope(nc, "ln1") as s:
        stats = s.sb("stats", [P, NP, 6])
        mean, rstd, tmp = s.sb("mean", [P, NP]), s.sb("rstd", [P, NP]), s.sb("tmp", [P, NP])
        steps, measured, variance, root = s.sem("steps"), s.sem("measured"), s.sem("variance"), s.sem("root")
        block = s.block()

        @block.vector
        def _(dve):
            step = Steps(dve, steps)
            with dve.Fori(0, NP) as t:
                nc.vector.bn_stats(stats[:, ds(t, 1), :].rearrange("p a b -> p (a b)"),
                                   agg[:, ds(t, 1), :].rearrange("p a b -> p (a b)")).then_inc(measured, 1)
            dve.wait_ge(measured, NP)
            layer_norm_scales(step, nc, c, stats, mean[:, :], rstd[:, :], tmp[:, :], lambda: dve.wait_ge(root, 1), variance)
            with dve.Fori(0, NP) as t:
                tile = agg[:, ds(t, 1), :].rearrange("p a b -> p (a b)")
                nc.vector.tensor_scalar(tile, tile, mean[:, ds(t, 1)], rstd[:, ds(t, 1)], ALU.subtract, ALU.mult)

        @block.scalar
        def _(act):
            act.wait_ge(variance, 1)
            nc.scalar.activation(tmp[:, :], tmp[:, :], ACT.Sqrt, bias=c["eps_ln"][:, :]).then_inc(root, 1)


_INS = ["x", "src", "dst", "edge_weight", "L0_gnn_W6", "L0_gnn_b6", "L0_gnn_W7", "L0_gnn_b7", "L0_gnn_Wp", "L0_gnn_bp",
        "L0_ffn_gate_w", "L0_ffn_gate_b", "L0_ffn_w1", "L0_ffn_b1", "L0_ffn_w2", "L0_ffn_b2", "L0_ffn_gamma", "L0_ffn_beta"]


def kernel(**inputs):
    import concourse.bacc as _bacc
    from concourse import mybir as _mybir
    from concourse.bass_utils import run_bass_kernel_spmd as _run

    nc = _bacc.Bacc("TRN2", target_bir_lowering=False, num_devices=1)
    arrays, args = {}, []
    for name in _INS:
        a = np.ascontiguousarray(inputs[name])
        arrays[f"in_{name}"] = a
        args.append(nc.dram_tensor(f"in_{name}", a.shape, _mybir.dt.from_np(a.dtype), kind="ExternalInput").ap())
    args.append(nc.dram_tensor("out_0", (NODES, D), _mybir.dt.float32, kind="ExternalOutput").ap())
    gnn_moe(nc, *args)
    r = _run(nc, [arrays], core_ids=[0])
    return r.results[0]["out_0"]
```
